# Optimizing a Trainium2 kernel written in Bass

```python
import numpy as np
import jax
import jax.numpy as jnp

def _softmax(x, axis=-1):
    return jax.nn.softmax(x, axis=axis)

def _gelu(x):
    return jax.nn.gelu(x, approximate=True)

def _silu(x):
    return jax.nn.silu(x)

def _sigmoid(x):
    return jax.nn.sigmoid(x)

def _layernorm(x, axis=-1, eps=1e-05):
    m = jnp.mean(x, axis=axis, keepdims=True)
    v = jnp.var(x, axis=axis, keepdims=True)
    return (x - m) / jnp.sqrt(v + eps)

def _scatter_add(tgt, idx, src, axis=0):
    return tgt.at[idx].add(src)

def _segment_sum(src, seg, n):
    return jax.ops.segment_sum(src, seg, n)
kernel_name = 'mk_rec_standalone_d1_rec_r8_db0c7b'

def setup_inputs(seed: int=0):
    np.random.seed(seed)
    _w = jnp.asarray

    def _rec_inputs():
        import jax
        import jax.numpy as jnp
        _rk = jax.random.key(seed)
        r_feature_emb = -0.000352921 + 0.999974 * jax.random.normal(jax.random.fold_in(_rk, 1), (512, 30, 128), jnp.float32)
        return r_feature_emb
    r_feature_emb = _rec_inputs()

    def _L0_rec_setup():
        import jax, jax.numpy as jnp
        import numpy as np
        from itertools import combinations
        key = jax.random.key(seed)
        k1, k2 = jax.random.split(key)
        B, F, D = (512, 30, 128)
        P = F * (F - 1) // 2
        feature_emb = jax.random.normal(k1, (B, F, D), dtype=jnp.float32)
        W = jax.random.normal(k2, (P, D, D), dtype=jnp.float32) * 0.02
        return {'feature_emb': feature_emb, 'W': W}
    _L0_rec_all = _L0_rec_setup()
    _L0_rec_in = {k: v for k, v in _L0_rec_all.items() if k in ('W',)}
    del _L0_rec_all
    return {'r_feature_emb': r_feature_emb, 'L0_rec_W': _L0_rec_in['W']}

def reference(r_feature_emb, L0_rec_W):
    import jax
    import jax.numpy as jnp

    def _L0_rec_ref(feature_emb, W):
        import jax, jax.numpy as jnp
        import numpy as np
        from itertools import combinations
        F = feature_emb.shape[1]
        pairs = np.array(list(combinations(range(F), 2)))
        idx_i = pairs[:, 0]
        idx_j = pairs[:, 1]
        v_i = feature_emb[:, idx_i]
        v_j = feature_emb[:, idx_j]
        proj = jnp.einsum('bpd,ped->bpe', v_i, W)
        return proj * v_j
    y = _L0_rec_ref(r_feature_emb, L0_rec_W)
    return y

_drawn_inputs = setup_inputs


def setup_inputs(seed=0):
    import zlib

    import numpy as np

    out = dict(_drawn_inputs(seed))
    spreads = {}
    factors = {}
    for name, (base, spread) in spreads.items():
        noise = np.random.default_rng([zlib.crc32(name.encode()), seed]).standard_normal(out[name].shape)
        drawn = base * np.exp(spread * noise) if base else spread * noise
        out[name] = jnp.asarray(drawn.astype(out[name].dtype))
    for name, factor in factors.items():
        out[name] = (out[name] * factor).astype(out[name].dtype)
    return out
```

```python
from contextlib import ExitStack

import concourse.bass as bass
from concourse import mybir

F32 = mybir.dt.float32
ALU = mybir.AluOpType

FIELDS = 30
BATCH = 512
DIM = 128

FOLDS = FIELDS // 2
SLOTS = FIELDS - 1
BANKS = 8
GROUPS = (5, 5, 5, 5, 4, 3, 2)
GROUP_START = [sum(GROUPS[:g]) for g in range(len(GROUPS))]
GROUP_END = [sum(GROUPS[:g + 1]) for g in range(len(GROUPS))]
X_PIECES = (1, 1, 2, 3, 4, 5, 7, 7)
X_START = [sum(X_PIECES[:n]) for n in range(len(X_PIECES))]

assert sum(GROUPS) == SLOTS and sum(X_PIECES) == FIELDS


def fold_pairs():
    return [[(r, r + 1 + s) if s < SLOTS - r else (SLOTS - r, s + 1) for s in range(SLOTS)]
            for r in range(FOLDS)]


def previous_in_bank(s):
    if s >= BANKS:
        return s - BANKS + 1
    return max(t for t in range(SLOTS) if t % BANKS == s) + 1 - SLOTS


def build(nc, xt_dram, w_dram, out_dram):
    with ExitStack() as ctx:
        xt = ctx.enter_context(nc.sbuf_tensor("xt", [DIM, FIELDS * BATCH], F32))
        w = ctx.enter_context(nc.sbuf_tensor("w", [DIM, SLOTS * DIM], F32))
        results = ctx.enter_context(nc.sbuf_tensor("results", [DIM, SLOTS * BATCH], F32))
        products = ctx.enter_context(nc.psum_tensor("products", [DIM, BANKS * BATCH], F32))

        x_loaded = [ctx.enter_context(nc.semaphore(f"x_loaded_{n}")) for n in range(len(X_PIECES))]
        w_loaded = [ctx.enter_context(nc.semaphore(f"w_loaded_{g}")) for g in range(len(GROUPS))]
        stored = [ctx.enter_context(nc.semaphore(f"stored_{g}")) for g in range(len(GROUPS))]
        projected = ctx.enter_context(nc.semaphore("projected"))
        multiplied = ctx.enter_context(nc.semaphore("multiplied"))

        block = ctx.enter_context(nc.Block())

        def w_group(g):
            return slice(GROUP_START[g] * DIM, GROUP_END[g] * DIM)

        def out_group(g):
            return slice(GROUP_START[g] * BATCH, GROUP_END[g] * BATCH)

        def a_field(value):
            return nc.s_assert_within(value, 0, FIELDS - 1,
                                      skip_runtime_bounds_check_because="it is r or SLOTS-r, or a j > i")

        def bank(s):
            return products[:, (s % BANKS) * BATCH:(s % BANKS + 1) * BATCH]

        @block.sync
        def _(sp):
            def load_x(n):
                cols = slice(X_START[n] * BATCH, (X_START[n] + X_PIECES[n]) * BATCH)
                sp.dma_start(xt[:, cols], xt_dram[:, cols]).then_inc(x_loaded[n], 16)

            for n in range(max(len(GROUPS), len(X_PIECES))):
                if n < len(X_PIECES):
                    load_x(n)
                if n < len(GROUPS):
                    sp.dma_start(w[:, w_group(n)], w_dram[0:DIM, w_group(n)]).then_inc(w_loaded[n], 16)
            with sp.Fori(1, FOLDS) as r:
                for g in range(len(GROUPS)):
                    sp.wait_ge(projected, (r - 1) * SLOTS + GROUP_END[g])
                    sp.dma_start(w[:, w_group(g)],
                                 w_dram[bass.ds(r * DIM, DIM), w_group(g)]).then_inc(w_loaded[g], 16)

        @block.tensor
        def _(pe):
            def project(s, moving_field):
                pe.matmul(bank(s), w[:, s * DIM:(s + 1) * DIM],
                          xt[:, bass.ds(moving_field * BATCH, BATCH)],
                          start=True, stop=True).then_inc(projected, 1)

            pe.wait_ge(x_loaded[0], 16)
            for s in range(SLOTS):
                if s in GROUP_START:
                    pe.wait_ge(w_loaded[GROUP_START.index(s)], 16)
                if s >= BANKS:
                    pe.wait_ge(multiplied, previous_in_bank(s))
                project(s, 0)
            for n in range(1, len(X_PIECES)):
                pe.wait_ge(x_loaded[n], 16)
            with pe.Fori(1, FOLDS) as r:
                for s in range(SLOTS):
                    if s in GROUP_START:
                        pe.wait_ge(w_loaded[GROUP_START.index(s)], 16 * r + 16)
                    pe.wait_ge(multiplied, r * SLOTS + previous_in_bank(s))
                    if s < FIELDS - FOLDS:
                        field = r
                    else:
                        folded = (r + s) // SLOTS
                        field = a_field(r + folded * (SLOTS - 2 * r))
                    project(s, field)

        @block.vector
        def _(dve):
            def multiply(s, field):
                dve.tensor_tensor(results[:, s * BATCH:(s + 1) * BATCH], bank(s),
                                  xt[:, bass.ds(field * BATCH, BATCH)],
                                  ALU.mult).then_inc(multiplied, 1)

            for s in range(SLOTS):
                if s + 1 in X_START:
                    dve.wait_ge(x_loaded[X_START.index(s + 1)], 16)
                dve.wait_ge(projected, s + 1)
                multiply(s, s + 1)
            with dve.Fori(1, FOLDS) as r:
                for s in range(SLOTS):
                    if s in GROUP_START:
                        dve.wait_ge(stored[GROUP_START.index(s)], 16 * r)
                    dve.wait_ge(projected, r * SLOTS + s + 1)
                    if s < FIELDS - FOLDS:
                        field = r + s + 1
                    else:
                        folded = (r + s) // SLOTS
                        field = a_field(s + 1 + r - folded * r)
                    multiply(s, field)

        @block.scalar
        def _(act):
            with act.Fori(0, FOLDS) as r:
                for g in range(len(GROUPS)):
                    act.wait_ge(multiplied, r * SLOTS + GROUP_END[g])
                    act.dma_start(out_dram[bass.ds(r * DIM, DIM), out_group(g)],
                                  results[:, out_group(g)]).then_inc(stored[g], 16)
            for g in range(len(GROUPS)):
                act.wait_ge(stored[g], 16 * FOLDS)


def kernel(r_feature_emb, L0_rec_W):
    import numpy as np
    import concourse.bacc as bacc
    from concourse.bass_utils import run_bass_kernel_spmd

    pair_index = {}
    for i in range(FIELDS):
        for j in range(i + 1, FIELDS):
            pair_index[(i, j)] = len(pair_index)
    order = np.array([[pair_index[pair] for pair in step] for step in fold_pairs()])

    x = np.asarray(r_feature_emb)
    w = np.asarray(L0_rec_W)
    xt = np.ascontiguousarray(x.transpose(2, 1, 0)).reshape(DIM, FIELDS * BATCH)
    wt = np.ascontiguousarray(w[order].transpose(0, 3, 1, 2)).reshape(FOLDS * DIM, SLOTS * DIM)

    nc = bacc.Bacc("TRN2", target_bir_lowering=False, num_devices=1)
    xt_dram = nc.dram_tensor("xt_dram", xt.shape, F32, kind="ExternalInput").ap()
    w_dram = nc.dram_tensor("w_dram", wt.shape, F32, kind="ExternalInput").ap()
    out_dram = nc.dram_tensor("out_dram", (FOLDS * DIM, SLOTS * BATCH), F32, kind="ExternalOutput").ap()
    build(nc, xt_dram, w_dram, out_dram)
    r = run_bass_kernel_spmd(nc, [{"xt_dram": xt, "w_dram": wt}], core_ids=[0])

    got = np.asarray(r.results[0]["out_dram"]).reshape(FOLDS, DIM, SLOTS, BATCH)
    out = np.empty((BATCH, len(pair_index), DIM), got.dtype)
    out[:, order.reshape(-1), :] = got.transpose(3, 0, 2, 1).reshape(BATCH, -1, DIM)
    return out
```
